# Optimizing a Trainium2 kernel written in Bass

```python
import numpy as np
import jax
import jax.numpy as jnp

def _softmax(x, axis=-1):
    return jax.nn.softmax(x, axis=axis)

def _gelu(x):
    return jax.nn.gelu(x, approximate=True)

def _silu(x):
    return jax.nn.silu(x)

def _sigmoid(x):
    return jax.nn.sigmoid(x)

def _layernorm(x, axis=-1, eps=1e-05):
    m = jnp.mean(x, axis=axis, keepdims=True)
    v = jnp.var(x, axis=axis, keepdims=True)
    return (x - m) / jnp.sqrt(v + eps)

def _scatter_add(tgt, idx, src, axis=0):
    return tgt.at[idx].add(src)

def _segment_sum(src, seg, n):
    return jax.ops.segment_sum(src, seg, n)
kernel_name = 'mk_dlrm_tower_d1_rec_r8_9b0e6f'

def setup_inputs(seed: int=0):
    np.random.seed(seed)
    _w = jnp.asarray

    def _rec_inputs():
        import jax
        import jax.numpy as jnp
        _tk = jax.random.key(seed)
        dense_ctx = jax.random.normal(jax.random.fold_in(_tk, 190), (512, 16), jnp.float32)
        ids = jnp.stack([jax.random.randint(jax.random.fold_in(_tk, 200 + f), (512,), 0, v, jnp.int32) for f, v in enumerate([1000, 1000, 125000, 12500, 12500, 125000, 1250, 12500, 125000, 1000, 1000, 1250, 1000, 12500, 1250, 1000, 1250, 12500, 1000, 1000, 1000, 12500, 1000, 1250, 12500, 1250, 1000, 12500, 1000, 1000, 1250, 1250])], axis=1)
        tbl_0 = 0.05 * jax.random.normal(jax.random.fold_in(_tk, 500 + 0), (1000, 64), jnp.float32)
        tbl_1 = 0.05 * jax.random.normal(jax.random.fold_in(_tk, 500 + 1), (1000, 64), jnp.float32)
        tbl_2 = 0.05 * jax.random.normal(jax.random.fold_in(_tk, 500 + 2), (125000, 64), jnp.float32)
        tbl_3 = 0.05 * jax.random.normal(jax.random.fold_in(_tk, 500 + 3), (12500, 64), jnp.float32)
        tbl_4 = 0.05 * jax.random.normal(jax.random.fold_in(_tk, 500 + 4), (12500, 64), jnp.float32)
        tbl_5 = 0.05 * jax.random.normal(jax.random.fold_in(_tk, 500 + 5), (125000, 64), jnp.float32)
        tbl_6 = 0.05 * jax.random.normal(jax.random.fold_in(_tk, 500 + 6), (1250, 64), jnp.float32)
        tbl_7 = 0.05 * jax.random.normal(jax.random.fold_in(_tk, 500 + 7), (12500, 64), jnp.float32)
        tbl_8 = 0.05 * jax.random.normal(jax.random.fold_in(_tk, 500 + 8), (125000, 64), jnp.float32)
        tbl_9 = 0.05 * jax.random.normal(jax.random.fold_in(_tk, 500 + 9), (1000, 64), jnp.float32)
        tbl_10 = 0.05 * jax.random.normal(jax.random.fold_in(_tk, 500 + 10), (1000, 64), jnp.float32)
        tbl_11 = 0.05 * jax.random.normal(jax.random.fold_in(_tk, 500 + 11), (1250, 64), jnp.float32)
        tbl_12 = 0.05 * jax.random.normal(jax.random.fold_in(_tk, 500 + 12), (1000, 64), jnp.float32)
        tbl_13 = 0.05 * jax.random.normal(jax.random.fold_in(_tk, 500 + 13), (12500, 64), jnp.float32)
        tbl_14 = 0.05 * jax.random.normal(jax.random.fold_in(_tk, 500 + 14), (1250, 64), jnp.float32)
        tbl_15 = 0.05 * jax.random.normal(jax.random.fold_in(_tk, 500 + 15), (1000, 64), jnp.float32)
        tbl_16 = 0.05 * jax.random.normal(jax.random.fold_in(_tk, 500 + 16), (1250, 64), jnp.float32)
        tbl_17 = 0.05 * jax.random.normal(jax.random.fold_in(_tk, 500 + 17), (12500, 64), jnp.float32)
        tbl_18 = 0.05 * jax.random.normal(jax.random.fold_in(_tk, 500 + 18), (1000, 64), jnp.float32)
        tbl_19 = 0.05 * jax.random.normal(jax.random.fold_in(_tk, 500 + 19), (1000, 64), jnp.float32)
        tbl_20 = 0.05 * jax.random.normal(jax.random.fold_in(_tk, 500 + 20), (1000, 64), jnp.float32)
        tbl_21 = 0.05 * jax.random.normal(jax.random.fold_in(_tk, 500 + 21), (12500, 64), jnp.float32)
        tbl_22 = 0.05 * jax.random.normal(jax.random.fold_in(_tk, 500 + 22), (1000, 64), jnp.float32)
        tbl_23 = 0.05 * jax.random.normal(jax.random.fold_in(_tk, 500 + 23), (1250, 64), jnp.float32)
        tbl_24 = 0.05 * jax.random.normal(jax.random.fold_in(_tk, 500 + 24), (12500, 64), jnp.float32)
        tbl_25 = 0.05 * jax.random.normal(jax.random.fold_in(_tk, 500 + 25), (1250, 64), jnp.float32)
        tbl_26 = 0.05 * jax.random.normal(jax.random.fold_in(_tk, 500 + 26), (1000, 64), jnp.float32)
        tbl_27 = 0.05 * jax.random.normal(jax.random.fold_in(_tk, 500 + 27), (12500, 64), jnp.float32)
        tbl_28 = 0.05 * jax.random.normal(jax.random.fold_in(_tk, 500 + 28), (1000, 64), jnp.float32)
        tbl_29 = 0.05 * jax.random.normal(jax.random.fold_in(_tk, 500 + 29), (1000, 64), jnp.float32)
        tbl_30 = 0.05 * jax.random.normal(jax.random.fold_in(_tk, 500 + 30), (1250, 64), jnp.float32)
        tbl_31 = 0.05 * jax.random.normal(jax.random.fold_in(_tk, 500 + 31), (1250, 64), jnp.float32)
        _rk = jax.random.fold_in(_tk, 7)
        W_top1 = 0.0441942 * jax.random.normal(jax.random.fold_in(_tk, 801), (512, 512), jnp.float32)
        W_top2 = 0.0441942 * jax.random.normal(jax.random.fold_in(_tk, 802), (512, 256), jnp.float32)
        W_top3 = 0.0625 * jax.random.normal(jax.random.fold_in(_tk, 803), (256, 1), jnp.float32)
        b_top1 = jnp.zeros((512,), jnp.float32)
        b_top2 = jnp.zeros((256,), jnp.float32)
        return (dense_ctx, ids, tbl_0, tbl_1, tbl_2, tbl_3, tbl_4, tbl_5, tbl_6, tbl_7, tbl_8, tbl_9, tbl_10, tbl_11, tbl_12, tbl_13, tbl_14, tbl_15, tbl_16, tbl_17, tbl_18, tbl_19, tbl_20, tbl_21, tbl_22, tbl_23, tbl_24, tbl_25, tbl_26, tbl_27, tbl_28, tbl_29, tbl_30, tbl_31, W_top1, b_top1, W_top2, b_top2, W_top3)
    dense_ctx, ids, tbl_0, tbl_1, tbl_2, tbl_3, tbl_4, tbl_5, tbl_6, tbl_7, tbl_8, tbl_9, tbl_10, tbl_11, tbl_12, tbl_13, tbl_14, tbl_15, tbl_16, tbl_17, tbl_18, tbl_19, tbl_20, tbl_21, tbl_22, tbl_23, tbl_24, tbl_25, tbl_26, tbl_27, tbl_28, tbl_29, tbl_30, tbl_31, W_top1, b_top1, W_top2, b_top2, W_top3 = _rec_inputs()

    def _L0_rec_setup():
        import jax, jax.numpy as jnp
        import numpy as np
        key = jax.random.key(seed)
        k1, k2 = jax.random.split(key)
        B, F, D = (512, 32, 64)
        P = F * (F - 1) // 2
        x = jax.random.normal(k1, (B, F, D), dtype=jnp.float32)
        W = jax.random.normal(k2, (P, D, D), dtype=jnp.float32) * (1.0 / np.sqrt(D))
        return {'x': x, 'W': W}
    _L0_rec_all = _L0_rec_setup()
    _L0_rec_in = {k: v for k, v in _L0_rec_all.items() if k in ('W',)}
    del _L0_rec_all
    return {'dense_ctx': dense_ctx, 'ids': ids, 'tbl_0': tbl_0, 'tbl_1': tbl_1, 'tbl_2': tbl_2, 'tbl_3': tbl_3, 'tbl_4': tbl_4, 'tbl_5': tbl_5, 'tbl_6': tbl_6, 'tbl_7': tbl_7, 'tbl_8': tbl_8, 'tbl_9': tbl_9, 'tbl_10': tbl_10, 'tbl_11': tbl_11, 'tbl_12': tbl_12, 'tbl_13': tbl_13, 'tbl_14': tbl_14, 'tbl_15': tbl_15, 'tbl_16': tbl_16, 'tbl_17': tbl_17, 'tbl_18': tbl_18, 'tbl_19': tbl_19, 'tbl_20': tbl_20, 'tbl_21': tbl_21, 'tbl_22': tbl_22, 'tbl_23': tbl_23, 'tbl_24': tbl_24, 'tbl_25': tbl_25, 'tbl_26': tbl_26, 'tbl_27': tbl_27, 'tbl_28': tbl_28, 'tbl_29': tbl_29, 'tbl_30': tbl_30, 'tbl_31': tbl_31, 'W_top1': W_top1, 'b_top1': b_top1, 'W_top2': W_top2, 'b_top2': b_top2, 'W_top3': W_top3, 'L0_rec_W': _L0_rec_in['W']}

def reference(dense_ctx, ids, tbl_0, tbl_1, tbl_2, tbl_3, tbl_4, tbl_5, tbl_6, tbl_7, tbl_8, tbl_9, tbl_10, tbl_11, tbl_12, tbl_13, tbl_14, tbl_15, tbl_16, tbl_17, tbl_18, tbl_19, tbl_20, tbl_21, tbl_22, tbl_23, tbl_24, tbl_25, tbl_26, tbl_27, tbl_28, tbl_29, tbl_30, tbl_31, W_top1, b_top1, W_top2, b_top2, W_top3, L0_rec_W):
    import jax
    import jax.numpy as jnp

    def _L0_rec_ref(x, W):
        import jax, jax.numpy as jnp
        import numpy as np
        F = x.shape[1]
        idx_i, idx_j = np.triu_indices(F, k=1)
        xi = x[:, idx_i, :]
        xj = x[:, idx_j, :]
        left = jnp.einsum('bpd,pde->bpe', xi, W)
        out = jnp.sum(left * xj, axis=-1)
        return out
    e = jnp.stack([tbl_0[ids[:, 0]], tbl_1[ids[:, 1]], tbl_2[ids[:, 2]], tbl_3[ids[:, 3]], tbl_4[ids[:, 4]], tbl_5[ids[:, 5]], tbl_6[ids[:, 6]], tbl_7[ids[:, 7]], tbl_8[ids[:, 8]], tbl_9[ids[:, 9]], tbl_10[ids[:, 10]], tbl_11[ids[:, 11]], tbl_12[ids[:, 12]], tbl_13[ids[:, 13]], tbl_14[ids[:, 14]], tbl_15[ids[:, 15]], tbl_16[ids[:, 16]], tbl_17[ids[:, 17]], tbl_18[ids[:, 18]], tbl_19[ids[:, 19]], tbl_20[ids[:, 20]], tbl_21[ids[:, 21]], tbl_22[ids[:, 22]], tbl_23[ids[:, 23]], tbl_24[ids[:, 24]], tbl_25[ids[:, 25]], tbl_26[ids[:, 26]], tbl_27[ids[:, 27]], tbl_28[ids[:, 28]], tbl_29[ids[:, 29]], tbl_30[ids[:, 30]], tbl_31[ids[:, 31]]], axis=1)
    z = _L0_rec_ref(e, L0_rec_W)
    z = z.reshape(z.shape[0], -1)
    h = jnp.concatenate([z, dense_ctx], axis=1)
    h = jnp.maximum(h @ W_top1 + b_top1, 0.0)
    h = jnp.maximum(h @ W_top2 + b_top2, 0.0)
    y = h @ W_top3
    return y

_drawn_inputs = setup_inputs


def setup_inputs(seed=0):
    import zlib

    import numpy as np

    out = dict(_drawn_inputs(seed))
    spreads = {'b_top1': (0.0, 0.1), 'b_top2': (0.0, 0.1)}
    factors = {}
    for name, (base, spread) in spreads.items():
        noise = np.random.default_rng([zlib.crc32(name.encode()), seed]).standard_normal(out[name].shape)
        drawn = base * np.exp(spread * noise) if base else spread * noise
        out[name] = jnp.asarray(drawn.astype(out[name].dtype))
    for name, factor in factors.items():
        out[name] = (out[name] * factor).astype(out[name].dtype)
    return out
```

```python
import concourse.bass as bass
from concourse import mybir
from contextlib import ExitStack

FP32 = mybir.dt.float32
INT32 = mybir.dt.int32
ALU = mybir.AluOpType
ACT = mybir.ActivationFunctionType

BATCH, TABLES, DIM, DENSE = 512, 32, 64, 16
PAIRS = TABLES // 2
HIDDEN1, HIDDEN2 = 512, 256
P = 128
BTILES = BATCH // P
ZTILES = 4
COLGROUPS = 4
UNITS_PER_ZTILE = 64
INTERACTIONS = TABLES * (TABLES - 1) // 2
UNITS = PAIRS * PAIRS
UNIT = 2 * DIM
CHUNK = 8 * UNIT


def weight_row(i, j):
    return i * (2 * TABLES - i - 1) // 2 + (j - i - 1)


def blocks():
    out, unit = [], 0
    for b in range(PAIRS):
        for a in range(b + 1):
            out.append((a, b, unit))
            unit += 1 if a == b else 2
    assert unit == UNITS == ZTILES * UNITS_PER_ZTILE
    return out


def z_place(unit):
    q, v = divmod(unit, UNITS_PER_ZTILE)
    return q, v % COLGROUPS, v // COLGROUPS


def layout():
    import numpy as np
    weights = np.full(UNITS * 2, -1)
    rows = np.zeros((ZTILES, P), np.int64)
    place = np.zeros((DENSE, ZTILES, P), np.float32)
    for a, b, unit in blocks():
        for s in range(1 if a == b else 2):
            q, cg, pos = z_place(unit + s)
            for h in range(2):
                row = 32 * cg + 2 * pos + h
                if a == b and h == 0:
                    rows[q, row] = INTERACTIONS + a
                    place[a, q, row] = 1.0
                else:
                    rows[q, row] = weight_row(2 * a + s, 2 * b + h)
                    weights[2 * (unit + s) + h] = rows[q, row]
    return weights, rows, place.reshape(DENSE, ZTILES * P)


def tower(nc, t, out):
    work = blocks()
    NB = len(work)
    CHUNKS = UNITS * UNIT // CHUNK
    NE, NW, NM = 4, 10, 3
    done_with = [max(k for k, (_, _, unit) in enumerate(work) if unit * UNIT // CHUNK <= c) for c in range(CHUNKS)]
    ends = [k for k, (a, b, unit) in enumerate(work) if unit % UNITS_PER_ZTILE + (1 if a == b else 2) >= UNITS_PER_ZTILE]

    with ExitStack() as ctx:
        def sb(name, shape, dt=FP32):
            return ctx.enter_context(nc.sbuf_tensor(name, shape, dt))

        def sem(name):
            return ctx.enter_context(nc.semaphore(name))

        ids = sb("ids", [P, BTILES, TABLES], INT32)
        emb = sb("emb", [P, NE, BTILES, P])
        embT = sb("embT", [P, PAIRS, BATCH])
        w = sb("w", [P, NW * CHUNK])
        prod = sb("prod", [P, NM, 2, BATCH])
        ident = sb("ident", [P, P])
        sel = sb("sel", [P, 16, 32])
        place = sb("place", [DENSE, ZTILES * P])
        denseT = sb("denseT", [DENSE, BATCH])
        zT = sb("zT", [P, ZTILES, BATCH])
        w1 = sb("w1", [P, ZTILES, HIDDEN1])
        w2 = sb("w2", [P, HIDDEN1 // P, HIDDEN2])
        w3 = sb("w3", [P, HIDDEN2 // P])
        b1 = sb("b1", [P, HIDDEN1 // P])
        b2 = sb("b2", [P, HIDDEN2 // P])
        h1 = sb("h1", [P, HIDDEN1 // P, BATCH])
        h2 = sb("h2", [P, HIDDEN2 // P, BATCH])
        y = sb("y", [1, BATCH])
        ps = ctx.enter_context(nc.psum_tensor("ps", [P, 8, BATCH], FP32))
        LEFT, TR, Z = [0, 2], [4, 5], [6, 7]

        ids_in = sem("ids_in")
        dense_in = sem("dense_in")
        top_in = sem("top_in")
        emb_in = [sem(f"emb_in{n}") for n in range(NE)]
        w_in = [sem(f"w_in{n}") for n in range(NW)]
        ident_set = sem("ident_set")
        sel_set = sem("sel_set")
        transposed = sem("transposed")
        embT_ready = sem("embT_ready")
        left_ready = sem("left_ready")
        prod_ready = sem("prod_ready")
        summed = sem("summed")
        zT_ready = sem("zT_ready")
        h1_done = sem("h1_done")
        h1_ready = sem("h1_ready")
        h2_done = sem("h2_done")
        h2_ready = sem("h2_ready")
        y_done = sem("y_done")
        y_ready = sem("y_ready")
        stored = sem("stored")

        block = ctx.enter_context(nc.Block())

        @block.sync
        def _(sp):
            sp.dma_start(ids[:, :, :], t["ids"]).then_inc(ids_in, 16)
            sp.dma_start(denseT[:, :], t["dense_ctx"]).then_inc(dense_in, 16)
            sp.dma_start(place[:, :], t["place"]).then_inc(dense_in, 16)
            for c in range(CHUNKS):
                if c >= NW:
                    sp.wait_ge(left_ready, done_with[c - NW] + 1)
                for s in range(2):
                    sp.dma_start(w[s * DIM:(s + 1) * DIM, (c % NW) * CHUNK:(c % NW + 1) * CHUNK],
                                 t["L0_rec_W"][:, c * CHUNK:(c + 1) * CHUNK]).then_inc(w_in[c % NW], 16)
                if c == NW:
                    sp.dma_start(w1[:, :, :], t["W_top1"]).then_inc(top_in, 16)
                    sp.dma_start(w2[:, :, :], t["W_top2"]).then_inc(top_in, 16)
                    sp.dma_start(w3[:, :], t["W_top3"]).then_inc(top_in, 16)
                    sp.dma_start(b1[:, :], t["b_top1"]).then_inc(top_in, 16)
                    sp.dma_start(b2[:, :], t["b_top2"]).then_inc(top_in, 16)
            sp.wait_ge(y_ready, 1)
            sp.dma_start(out, y[:, :]).then_inc(stored, 16)
            sp.wait_ge(stored, 16)

        @block.gpsimd
        def _(pool):
            nc.gpsimd.memset(ident[:, :], 0.0).then_inc(ident_set, 1)
            pool.wait_ge(ident_set, 1)
            nc.gpsimd.affine_select(out=ident[:, :], in_=ident[:, :], compare_op=ALU.not_equal, fill=1.0, base=0,
                                    pattern=[[-1, P]], channel_multiplier=1).then_inc(ident_set, 1)
            pool.wait_ge(ids_in, 16)
            for b in range(PAIRS):
                if b >= NE:
                    pool.wait_ge(transposed, b - NE + 1)
                for f in (2 * b, 2 * b + 1):
                    for n in range(BTILES):
                        nc.gpsimd.indirect_dma_start(
                            out=emb[:, b % NE, n, (f % 2) * DIM:(f % 2 + 1) * DIM], out_offset=None,
                            in_=t[f"tbl_{f}"],
                            in_offset=bass.IndirectOffsetOnAxis(ap=ids[:, n, f:f + 1], axis=0),
                        ).then_inc(emb_in[b % NE], 16)

        @block.tensor
        def _(pe):
            def transpose_pair(b):
                pe.wait_ge(emb_in[b % NE], 16 * 2 * BTILES * (b // NE + 1))
                if b >= 2:
                    pe.wait_ge(embT_ready, b - 1)
                for n in range(BTILES):
                    last = nc.tensor.transpose(ps[:, TR[b % 2], n * P:(n + 1) * P], emb[:, b % NE, n, :], ident[:, :])
                last.then_inc(transposed, 1)

            def left(k):
                a, b, unit = work[k]
                pe.wait_ge(embT_ready, b + 1)
                if k >= 2:
                    pe.wait_ge(prod_ready, k - 1)
                bank = LEFT[k % 2]
                for s in range(1 if a == b else 2):
                    c, at = divmod((unit + s) * UNIT, CHUNK)
                    pe.wait_ge(w_in[c % NW], 32 * (c // NW + 1))
                    at += (c % NW) * CHUNK
                    r = slice(s * DIM, (s + 1) * DIM)
                    last = nc.tensor.matmul(ps[:, bank + s, :], w[r, at:at + UNIT], embT[r, a, :],
                                            start=True, stop=True)
                last.then_inc(left_ready, 1)

            opened = set()

            def total(k):
                a, b, unit = work[k]
                pe.wait_ge(prod_ready, k + 1)
                for s in range(1 if a == b else 2):
                    q, cg, pos = z_place(unit + s)
                    if q not in opened:
                        opened.add(q)
                        if q >= 2:
                            pe.wait_ge(zT_ready, q - 1)
                        nc.tensor.matmul(ps[:, Z[q % 2], :], place[:, q * P:(q + 1) * P], denseT[:, :],
                                         start=True, stop=False, skip_group_check=True)
                    r = slice(DIM, P) if a == b else slice(0, P)
                    last = nc.tensor.matmul(ps[32 * cg:32 * cg + 32, Z[q % 2], :], sel[r, pos, :],
                                            prod[r, k % NM, s, :], start=False, stop=pos == 15, skip_group_check=True)
                last.then_inc(summed, 1)

            pe.wait_ge(ident_set, 2)
            pe.wait_ge(sel_set, 3)
            pe.wait_ge(dense_in, 32)
            there = 0
            for k in range(NB + 2):
                if k < NB:
                    while there <= work[k][1]:
                        transpose_pair(there)
                        there += 1
                    left(k)
                if k >= 2:
                    total(k - 2)

            pe.wait_ge(top_in, 80)
            pe.wait_ge(zT_ready, ZTILES)
            for m in range(HIDDEN1 // P):
                for q in range(ZTILES):
                    last = nc.tensor.matmul(ps[:, m, :], w1[:, q, m * P:(m + 1) * P], zT[:, q, :],
                                            start=q == 0, stop=q == ZTILES - 1)
                last.then_inc(h1_done, 1)
            for m in range(HIDDEN2 // P):
                for q in range(HIDDEN1 // P):
                    pe.wait_ge(h1_ready, q + 1)
                    last = nc.tensor.matmul(ps[:, 4 + m, :], w2[:, q, m * P:(m + 1) * P], h1[:, q, :],
                                            start=q == 0, stop=q == HIDDEN1 // P - 1)
                last.then_inc(h2_done, 1)
            for q in range(HIDDEN2 // P):
                pe.wait_ge(h2_ready, q + 1)
                last = nc.tensor.matmul(ps[0:1, 6, :], w3[:, q:q + 1], h2[:, q, :],
                                        start=q == 0, stop=q == HIDDEN2 // P - 1)
            last.then_inc(y_done, 1)

        @block.vector
        def _(dve):
            nc.vector.memset(sel[:, :, :], 0.0).then_inc(sel_set, 1)
            dve.wait_ge(sel_set, 1)
            flat = sel[:, :, :].rearrange("p a c -> p (a c)")
            nc.vector.memset(flat[0:DIM, 0:511:34], 1.0).then_inc(sel_set, 1)
            nc.vector.memset(flat[DIM:P, 1:512:34], 1.0).then_inc(sel_set, 1)
            for k, (a, b, unit) in enumerate(work):
                dve.wait_ge(left_ready, k + 1)
                if k >= NM:
                    dve.wait_ge(summed, k - NM + 1)
                bank = LEFT[k % 2]
                if a == b:
                    nc.vector.tensor_tensor(prod[DIM:P, k % NM, 0, :], ps[DIM:P, bank, :], embT[DIM:P, b, :],
                                            ALU.mult).then_inc(prod_ready, 1)
                else:
                    nc.vector.tensor_tensor(prod[:, k % NM, :, :], ps[:, bank:bank + 2, :],
                                            embT[:, b:b + 1, :].broadcast_to([P, 2, BATCH]),
                                            ALU.mult).then_inc(prod_ready, 1)
            dve.wait_ge(y_done, 1)
            nc.vector.tensor_copy(y[:, :], ps[0:1, 6, :]).then_inc(y_ready, 1)

        @block.scalar
        def _(act):
            def z_out(q):
                act.wait_ge(summed, ends[q] + 1)
                nc.scalar.copy(zT[:, q, :], ps[:, Z[q % 2], :]).then_inc(zT_ready, 1)

            q = 0
            for b in range(PAIRS):
                act.wait_ge(transposed, b + 1)
                nc.scalar.copy(embT[:, b, :], ps[:, TR[b % 2], :]).then_inc(embT_ready, 1)
                while q < ZTILES - 1 and max(x[1] for x in work[:ends[q] + 3]) <= b:
                    z_out(q)
                    q += 1
            for q in range(q, ZTILES):
                z_out(q)
            act.wait_ge(top_in, 80)
            for m in range(HIDDEN1 // P):
                act.wait_ge(h1_done, m + 1)
                nc.scalar.activation(h1[:, m, :], ps[:, m, :], ACT.Relu, bias=b1[:, m:m + 1]).then_inc(h1_ready, 1)
            for m in range(HIDDEN2 // P):
                act.wait_ge(h2_done, m + 1)
                nc.scalar.activation(h2[:, m, :], ps[:, 4 + m, :], ACT.Relu, bias=b2[:, m:m + 1]).then_inc(h2_ready, 1)


def kernel(**inputs):
    import numpy as np
    import concourse.bacc as bacc
    from concourse.bass_utils import run_bass_kernel_spmd

    def tiled(a):
        a = a.reshape(-1, P, a.shape[-1])
        return a.transpose(1, 0, 2)

    nc = bacc.Bacc("TRN2", target_bir_lowering=False, num_devices=1)
    weights, rows, place = layout()
    x = {name: np.asarray(a) for name, a in inputs.items()}
    arrays = {f"tbl_{f}": x[f"tbl_{f}"] for f in range(TABLES)}
    arrays["ids"] = tiled(x["ids"])
    arrays["dense_ctx"] = x["dense_ctx"].T
    w = np.zeros((DIM, 2 * UNITS, DIM), x["L0_rec_W"].dtype)
    w[:, weights >= 0] = x["L0_rec_W"][weights[weights >= 0]].transpose(1, 0, 2)
    arrays["L0_rec_W"] = w.reshape(DIM, UNITS * UNIT)
    arrays["W_top1"] = tiled(x["W_top1"][rows.reshape(-1)])
    arrays["W_top2"] = tiled(x["W_top2"])
    arrays["W_top3"] = x["W_top3"].reshape(-1, P).T
    arrays["b_top1"] = x["b_top1"].reshape(-1, P).T
    arrays["b_top2"] = x["b_top2"].reshape(-1, P).T
    arrays["place"] = place
    arrays = {name: np.ascontiguousarray(a) for name, a in arrays.items()}
    t = {name: nc.dram_tensor(f"in_{name}", a.shape, mybir.dt.from_np(a.dtype), kind="ExternalInput").ap()
         for name, a in arrays.items()}
    out = nc.dram_tensor("out_y", (1, BATCH), FP32, kind="ExternalOutput").ap()
    tower(nc, t, out)
    r = run_bass_kernel_spmd(nc, [{f"in_{name}": a for name, a in arrays.items()}], core_ids=[0])
    return r.results[0]["out_y"].reshape(BATCH, 1)
```

```python
import concourse.bass as bass
from concourse import mybir
from contextlib import ExitStack

FP32 = mybir.dt.float32
FP32R = mybir.dt.float32r
INT32 = mybir.dt.int32
ALU = mybir.AluOpType
ACT = mybir.ActivationFunctionType

BATCH, TABLES, DIM, DENSE = 512, 32, 64, 16
PAIRS = TABLES // 2
HIDDEN1, HIDDEN2 = 512, 256
P = 128
BTILES = BATCH // P
ZTILES = 4
COLGROUPS = 4
UNITS_PER_ZTILE = 64
INTERACTIONS = TABLES * (TABLES - 1) // 2
UNITS = PAIRS * PAIRS
UNIT = 2 * DIM
CHUNK = 8 * UNIT


def weight_row(i, j):
    return i * (2 * TABLES - i - 1) // 2 + (j - i - 1)


def blocks():
    out, unit = [], 0
    for b in range(PAIRS):
        odd_end = b % 2 and unit // UNITS_PER_ZTILE != (unit + 2 * b) // UNITS_PER_ZTILE
        for a in ([b] + list(range(b)) if odd_end else range(b + 1)):
            out.append((a, b, unit))
            unit += 1 if a == b else 2
    assert unit == UNITS == ZTILES * UNITS_PER_ZTILE
    return out


def z_place(unit):
    q, v = divmod(unit, UNITS_PER_ZTILE)
    return q, v % COLGROUPS, v // COLGROUPS


def layout():
    import numpy as np
    weights = np.full(UNITS * 2, -1)
    rows = np.zeros((ZTILES, P), np.int64)
    place = np.zeros((DIM, ZTILES, P), np.float32)
    for a, b, unit in blocks():
        for s in range(1 if a == b else 2):
            q, cg, pos = z_place(unit + s)
            for h in range(2):
                row = 32 * cg + 2 * pos + h
                if a == b and h == 0:
                    rows[q, row] = INTERACTIONS + a
                    place[a, q, row] = place[DIM // 2 + a, q, row] = 1.0
                else:
                    rows[q, row] = weight_row(2 * a + s, 2 * b + h)
                    weights[2 * (unit + s) + h] = rows[q, row]
    return weights, rows, place.reshape(DIM, ZTILES * P)


def tower(nc, t, out):
    work = blocks()
    NB = len(work)
    CHUNKS = UNITS * UNIT // CHUNK
    NE, NR, NW, NL, NM = 4, 3, 6, 3, 4
    LAG = 4
    done_with = [max(k for k, (_, _, unit) in enumerate(work) if unit * UNIT // CHUNK <= c) for c in range(CHUNKS)]
    ends = [k for k, (a, b, unit) in enumerate(work) if (unit + (1 if a == b else 2)) % UNITS_PER_ZTILE == 0]
    SLOW, EARLIER = 8, 4
    stage = [b * (b + 1) // 2 for b in range(PAIRS)]
    after = [stage[b] - 1 - (EARLIER if b >= SLOW else 0) for b in range(PAIRS)]
    DVE_CHUNKS = 10
    AHEAD = 6
    needed = [min(k for k, (_, _, unit) in enumerate(work) if (unit + 1) * UNIT // CHUNK >= c) for c in range(CHUNKS)]
    pool_order = sorted([(after[b], 0, b) for b in range(PAIRS)]
                        + [(needed[c] - AHEAD, 1, c) for c in range(DVE_CHUNKS, CHUNKS)])
    early = [max(ends[ZTILES - 2] + LAG, after[-1]) + 4 + 3 * m for m in range(HIDDEN1 // P)]

    def due(k):
        return [b for b in range(PAIRS) if after[b] == k]

    def lo_due(k):
        return [(b, h) for b in range(1, PAIRS) for h in range(2)
                if k == (stage[b] if b < SLOW else after[b] + 1 + h)]

    def sums_due(k):
        if k == NB - 1:
            return range((k - 1) // 2 * 2 - LAG + 2, NB)
        return range(k - LAG, k - LAG + 2) if k % 2 == 0 and k >= LAG else range(0)

    def chunks_due(k):
        return [c for c in range(CHUNKS) if (done_with[c - NW] if c >= NW else -1) == k]

    with ExitStack() as ctx:
        def sb(name, shape, dt=FP32):
            return ctx.enter_context(nc.sbuf_tensor(name, shape, dt))

        def sem(name):
            return ctx.enter_context(nc.semaphore(name))

        ids = sb("ids", [P, BTILES, TABLES], INT32)
        emb = sb("emb", [P, NE, BTILES, P])
        embT = sb("embT", [P, PAIRS, BATCH])
        embHL = sb("embHL", [P, TABLES, BATCH], FP32R)
        w = sb("w", [P, NR, CHUNK])
        wH = sb("wH", [P, NW, CHUNK], FP32R)
        wL = sb("wL", [P, NW, CHUNK], FP32R)
        prod = sb("prod", [P, NM, 2, BATCH])
        dense = prod[0:DENSE, NM - 1, 0, :]
        place = prod[0:DIM, NM - 1, 1, :]
        ident = sb("ident", [P, P])
        sel = sb("sel", [P, 16, 32])
        denseHL = sb("denseHL", [DIM, BATCH], FP32R)
        placeR = sb("placeR", [DIM, ZTILES * P], FP32R)
        zT = sb("zT", [P, ZTILES, BATCH])
        w1 = sb("w1", [P, ZTILES, HIDDEN1])
        w2 = sb("w2", [P, HIDDEN1 // P, HIDDEN2])
        w3 = sb("w3", [P, HIDDEN2 // P])
        b1 = sb("b1", [P, HIDDEN1 // P])
        b2 = sb("b2", [P, HIDDEN2 // P])
        h1 = embT[:, 0:HIDDEN1 // P, :]
        h2 = embT[:, HIDDEN1 // P:(HIDDEN1 + HIDDEN2) // P, :]
        y = sb("y", [P, BTILES])
        h1_part = emb[:, :, :, :].rearrange("p s n c -> p s (n c)")
        ps = ctx.enter_context(nc.psum_tensor("ps", [P, 8, BATCH], FP32))
        LEFT, TR, Z = [0, 2, 4], 6, 7

        ids_in = sem("ids_in")
        dense_in = sem("dense_in")
        top_in = sem("top_in")
        emb_in = [sem(f"emb_in{n}") for n in range(NE)]
        w_in = [sem(f"w_in{n}") for n in range(NR)]
        ident_set = sem("ident_set")
        sel_set = sem("sel_set")
        cleared = sem("cleared")
        denseH_ready = sem("denseH_ready")
        denseHL_ready = sem("denseHL_ready")
        wH_ready = sem("wH_ready")
        wL_dve = sem("wL_dve")
        wL_pool = sem("wL_pool")
        transposed = sem("transposed")
        embT_ready = sem("embT_ready")
        embLo_ready = sem("embLo_ready")
        left_ready = sem("left_ready")
        prod_ready = sem("prod_ready")
        summed = sem("summed")
        zT_ready = sem("zT_ready")
        part_done = sem("part_done")
        part_ready = sem("part_ready")
        h1_done = sem("h1_done")
        h1_added = sem("h1_added")
        h1_ready = sem("h1_ready")
        h2_done = sem("h2_done")
        h2_ready = sem("h2_ready")
        y_done = sem("y_done")
        y_ready = sem("y_ready")
        stored = sem("stored")

        block = ctx.enter_context(nc.Block())

        def wait_split(eng, c):
            if c < DVE_CHUNKS:
                eng.wait_ge(wL_dve, c + 1)
            else:
                eng.wait_ge(wL_pool, c - DVE_CHUNKS + 1)

        @block.sync
        def _(sp):
            sp.dma_start(ids[:, :, :], t["ids"]).then_inc(ids_in, 16)

            def load(c, slot):
                for s in range(2):
                    sp.dma_start(w[s * DIM:(s + 1) * DIM, slot, :],
                                 t["L0_rec_W"][:, bass.ds(c * CHUNK, CHUNK)]).then_inc(w_in[slot], 16)

            for c in range(DVE_CHUNKS + NR):
                if c >= NR:
                    sp.wait_ge(wL_dve, c - NR + 1)
                load(c, c % NR)
                if c == 0:
                    sp.dma_start(dense, t["dense_ctx"]).then_inc(dense_in, 16)
                    sp.dma_start(place, t["place"]).then_inc(dense_in, 16)
                if c == NW:
                    sp.dma_start(w1[:, :, :], t["W_top1"]).then_inc(top_in, 16)
                    sp.dma_start(w2[:, :, :], t["W_top2"]).then_inc(top_in, 16)
                    sp.dma_start(w3[:, :], t["W_top3"]).then_inc(top_in, 16)
                    sp.dma_start(b1[:, :], t["b_top1"]).then_inc(top_in, 16)
                    sp.dma_start(b2[:, :], t["b_top2"]).then_inc(top_in, 16)
            first = DVE_CHUNKS + NR
            rounds = (CHUNKS - first) // NR
            with sp.Fori(0, rounds, 1) as turn:
                for n in range(NR):
                    sp.wait_ge(wL_pool, turn * NR + (n + 1))
                    load(turn * NR + (first + n), (first + n) % NR)
            for c in range(first + NR * rounds, CHUNKS):
                sp.wait_ge(wL_pool, c - NR - DVE_CHUNKS + 1)
                load(c, c % NR)
            sp.wait_ge(y_ready, 1)
            sp.dma_start(out, y[:, :]).then_inc(stored, 16)
            sp.wait_ge(stored, 16)

        @block.gpsimd
        def _(pool):
            nc.gpsimd.memset(ident[:, :], 0.0).then_inc(ident_set, 1)
            pool.wait_ge(ident_set, 1)
            nc.gpsimd.affine_select(out=ident[:, :], in_=ident[:, :], compare_op=ALU.not_equal, fill=1.0, base=0,
                                    pattern=[[-1, P]], channel_multiplier=1).then_inc(ident_set, 1)
            pool.wait_ge(ids_in, 16)

            def gather(b):
                if b >= NE:
                    pool.wait_ge(transposed, b - NE + 1)
                for f in (2 * b, 2 * b + 1):
                    for n in range(BTILES):
                        nc.gpsimd.indirect_dma_start(
                            out=emb[:, b % NE, n, (f % 2) * DIM:(f % 2 + 1) * DIM], out_offset=None,
                            in_=t[f"tbl_{f}"],
                            in_offset=bass.IndirectOffsetOnAxis(ap=ids[:, n, f:f + 1], axis=0),
                        ).then_inc(emb_in[b % NE], 16)

            def weights_lo(c):
                pool.wait_ge(wH_ready, c + 1)
                pool.wait_ge(left_ready, done_with[c - NW] + 1)
                nc.gpsimd.tensor_tensor(wL[:, c % NW, :], w[:, c % NR, :], wH[:, c % NW, :].bitcast(FP32),
                                        ALU.subtract).then_inc(wL_pool, 1)

            for _, weights, n in pool_order:
                if weights:
                    weights_lo(n)
                else:
                    gather(n)

        @block.tensor
        def _(pe):
            def transpose_pair(b):
                pe.wait_ge(emb_in[b % NE], 16 * 2 * BTILES * (b // NE + 1))
                if b >= 1:
                    pe.wait_ge(embLo_ready, 2 * b)
                for n in range(BTILES):
                    last = nc.tensor.transpose(ps[:, TR, n * P:(n + 1) * P], emb[:, b % NE, n, :], ident[:, :])
                last.then_inc(transposed, 1)

            def left(k):
                a, b, unit = work[k]
                pe.wait_ge(embLo_ready, 2 * (a + 1))
                if k >= NL:
                    pe.wait_ge(prod_ready, k - NL + 1)
                for s in range(1 if a == b else 2):
                    c, at = divmod((unit + s) * UNIT, CHUNK)
                    wait_split(pe, c)
                    for n, part in enumerate((wH, wL)):
                        last = nc.tensor.matmul(ps[:, LEFT[k % NL] + s, :], part[:, c % NW, at:at + UNIT],
                                                embHL[:, 2 * a + s, :], start=n == 0, stop=n == 1)
                last.then_inc(left_ready, 1)

            opened = set()

            def total(k):
                a, b, unit = work[k]
                pe.wait_ge(prod_ready, k + 1)
                for s in range(1 if a == b else 2):
                    q, cg, pos = z_place(unit + s)
                    if q not in opened:
                        opened.add(q)
                        if q >= 1:
                            pe.wait_ge(zT_ready, q)
                        nc.tensor.matmul(ps[:, Z, :], placeR[:, q * P:(q + 1) * P], denseHL[:, :],
                                         start=True, stop=False, skip_group_check=True)
                    r = slice(DIM, P) if a == b else slice(0, P)
                    last = nc.tensor.matmul(ps[32 * cg:32 * cg + 32, Z, :], sel[r, pos, :],
                                            prod[r, k % NM, s, :], start=False, stop=pos == 15, skip_group_check=True)
                last.then_inc(summed, 1)

            pe.wait_ge(ident_set, 2)
            pe.wait_ge(sel_set, 3)
            pe.wait_ge(denseHL_ready, 1)
            pe.wait_ge(denseH_ready, 2)
            transpose_pair(0)
            for k in range(NB):
                left(k)
                for m in sums_due(k):
                    total(m)
                for b in due(k):
                    transpose_pair(b)
                if k in early:
                    m = early.index(k)
                    if m == 0:
                        pe.wait_ge(top_in, 80)
                        pe.wait_ge(zT_ready, ZTILES - 1)
                        pe.wait_ge(embLo_ready, TABLES)
                    else:
                        pe.wait_ge(part_ready, m)
                    for q in range(ZTILES - 1):
                        last = nc.tensor.matmul(ps[:, TR, :], w1[:, q, m * P:(m + 1) * P], zT[:, q, :],
                                                start=q == 0, stop=q == ZTILES - 2)
                    last.then_inc(part_done, 1)

            pe.wait_ge(zT_ready, ZTILES)
            for m in range(HIDDEN1 // P):
                nc.tensor.matmul(ps[:, m, :], w1[:, ZTILES - 1, m * P:(m + 1) * P], zT[:, ZTILES - 1, :],
                                 start=True, stop=True).then_inc(h1_done, 1)
            for q in range(HIDDEN1 // P):
                pe.wait_ge(h1_ready, q + 1)
                for m in range(HIDDEN2 // P):
                    last = nc.tensor.matmul(ps[:, 4 + m, :], w2[:, q, m * P:(m + 1) * P], h1[:, q, :],
                                            start=q == 0, stop=q == HIDDEN1 // P - 1)
                    if q == HIDDEN1 // P - 1:
                        last.then_inc(h2_done, 1)
            pe.wait_ge(h2_ready, HIDDEN2 // P)
            for n in range(BTILES):
                for q in range(HIDDEN2 // P):
                    last = nc.tensor.matmul(ps[:, 6, n:n + 1], h2[:, q, n * P:(n + 1) * P], w3[:, q:q + 1],
                                            start=q == 0, stop=q == HIDDEN2 // P - 1)
            last.then_inc(y_done, 1)

        @block.vector
        def _(dve):
            def weights_lo(c):
                dve.wait_ge(wH_ready, c + 1)
                if c >= NW:
                    dve.wait_ge(left_ready, done_with[c - NW] + 1)
                nc.vector.tensor_tensor(wL[:, c % NW, :], w[:, c % NR, :], wH[:, c % NW, :].bitcast(FP32),
                                        ALU.subtract).then_inc(wL_dve, 1)

            def table_lo(b, h):
                dve.wait_ge(embT_ready, 3 * b + 2 + h)
                here, there = slice(h * DIM, (h + 1) * DIM), slice((1 - h) * DIM, (2 - h) * DIM)
                nc.vector.tensor_tensor(embHL[there, 2 * b + h, :], ps[here, TR, :],
                                        embHL[here, 2 * b + h, :].bitcast(FP32),
                                        ALU.subtract).then_inc(embLo_ready, 1)

            nc.vector.memset(denseHL[:, :].bitcast(FP32), 0.0).then_inc(cleared, 1)
            nc.vector.memset(sel[:, :, :], 0.0).then_inc(sel_set, 1)
            dve.wait_ge(sel_set, 1)
            flat = sel[:, :, :].rearrange("p a c -> p (a c)")
            nc.vector.memset(flat[0:DIM, 0:511:34], 1.0).then_inc(sel_set, 1)
            nc.vector.memset(flat[DIM:P, 1:512:34], 1.0).then_inc(sel_set, 1)
            dve.wait_ge(denseH_ready, 1)
            nc.vector.tensor_tensor(denseHL[DIM // 2:DIM // 2 + DENSE, :], dense,
                                    denseHL[0:DENSE, :].bitcast(FP32), ALU.subtract).then_inc(denseHL_ready, 1)
            for c in chunks_due(-1):
                weights_lo(c)
            for h in range(2):
                table_lo(0, h)
            for k, (a, b, unit) in enumerate(work):
                dve.wait_ge(left_ready, k + 1)
                if k >= NM:
                    dve.wait_ge(summed, k - NM + 1)
                dve.wait_ge(embT_ready, 3 * b + 1)
                bank = LEFT[k % NL]
                if a == b:
                    nc.vector.tensor_tensor(prod[DIM:P, k % NM, 0, :], ps[DIM:P, bank, :], embT[DIM:P, b, :],
                                            ALU.mult).then_inc(prod_ready, 1)
                else:
                    nc.vector.tensor_tensor(prod[:, k % NM, :, :], ps[:, bank:bank + 2, :],
                                            embT[:, b:b + 1, :].broadcast_to([P, 2, BATCH]),
                                            ALU.mult).then_inc(prod_ready, 1)
                for n, h in lo_due(k):
                    table_lo(n, h)
                for c in chunks_due(k):
                    if c < DVE_CHUNKS:
                        weights_lo(c)
            for m in range(HIDDEN1 // P):
                dve.wait_ge(h1_done, m + 1)
                if m == 0:
                    dve.wait_ge(part_ready, HIDDEN1 // P)
                nc.vector.tensor_tensor(h1_part[:, m, :], ps[:, m, :], h1_part[:, m, :], ALU.add).then_inc(h1_added, 1)
            dve.wait_ge(y_done, 1)
            nc.vector.tensor_copy(y[:, :], ps[:, 6, 0:BTILES]).then_inc(y_ready, 1)

        @block.scalar
        def _(act):
            def weights_hi(c):
                act.wait_ge(w_in[c % NR], 32 * (c // NR + 1))
                if c >= NW:
                    act.wait_ge(left_ready, done_with[c - NW] + 1)
                nc.scalar.copy(wH[:, c % NW, :], w[:, c % NR, :]).then_inc(wH_ready, 1)

            def pair_out(b):
                act.wait_ge(transposed, b + 1)
                nc.scalar.copy(embT[:, b, :], ps[:, TR, :]).then_inc(embT_ready, 1)
                for h in range(2):
                    here = slice(h * DIM, (h + 1) * DIM)
                    nc.scalar.copy(embHL[here, 2 * b + h, :], ps[here, TR, :]).then_inc(embT_ready, 1)

            def z_out(q):
                act.wait_ge(summed, ends[q] + 1)
                nc.scalar.copy(zT[:, q, :], ps[:, Z, :]).then_inc(zT_ready, 1)

            act.wait_ge(dense_in, 32)
            act.wait_ge(cleared, 1)
            nc.scalar.copy(denseHL[0:DENSE, :], dense).then_inc(denseH_ready, 1)
            nc.scalar.copy(placeR[:, :], place).then_inc(denseH_ready, 1)
            for c in chunks_due(-1):
                weights_hi(c)
            pair_out(0)
            for k in range(NB):
                for q in range(ZTILES - 1):
                    if ends[q] in sums_due(k):
                        z_out(q)
                for b in due(k):
                    pair_out(b)
                for c in chunks_due(k):
                    weights_hi(c)
                if k in early:
                    m = early.index(k)
                    if m == 0:
                        act.wait_ge(top_in, 80)
                    act.wait_ge(part_done, m + 1)
                    nc.scalar.activation(h1_part[:, m, :], ps[:, TR, :], ACT.Identity,
                                         bias=b1[:, m:m + 1]).then_inc(part_ready, 1)
            z_out(ZTILES - 1)
            for m in range(HIDDEN1 // P):
                act.wait_ge(h1_added, m + 1)
                nc.scalar.activation(h1[:, m, :], h1_part[:, m, :], ACT.Relu).then_inc(h1_ready, 1)
            for m in range(HIDDEN2 // P):
                act.wait_ge(h2_done, m + 1)
                nc.scalar.activation(h2[:, m, :], ps[:, 4 + m, :], ACT.Relu, bias=b2[:, m:m + 1]).then_inc(h2_ready, 1)


def kernel(**inputs):
    import numpy as np
    import concourse.bacc as bacc
    from concourse.bass_utils import run_bass_kernel_spmd

    def tiled(a):
        a = a.reshape(-1, P, a.shape[-1])
        return a.transpose(1, 0, 2)

    nc = bacc.Bacc("TRN2", target_bir_lowering=False, num_devices=1)
    weights, rows, place = layout()
    x = {name: np.asarray(a) for name, a in inputs.items()}
    arrays = {f"tbl_{f}": x[f"tbl_{f}"] for f in range(TABLES)}
    arrays["ids"] = tiled(x["ids"])
    arrays["dense_ctx"] = x["dense_ctx"].T
    w = np.zeros((DIM, 2 * UNITS, DIM), x["L0_rec_W"].dtype)
    w[:, weights >= 0] = x["L0_rec_W"][weights[weights >= 0]].transpose(1, 0, 2)
    arrays["L0_rec_W"] = w.reshape(DIM, UNITS * UNIT)
    arrays["W_top1"] = tiled(x["W_top1"][rows.reshape(-1)])
    arrays["W_top2"] = tiled(x["W_top2"])
    arrays["W_top3"] = x["W_top3"].reshape(-1, P).T
    arrays["b_top1"] = x["b_top1"].reshape(-1, P).T
    arrays["b_top2"] = x["b_top2"].reshape(-1, P).T
    arrays["place"] = place
    arrays = {name: np.ascontiguousarray(a) for name, a in arrays.items()}
    t = {name: nc.dram_tensor(f"in_{name}", a.shape, mybir.dt.from_np(a.dtype), kind="ExternalInput").ap()
         for name, a in arrays.items()}
    out = nc.dram_tensor("out_y", (P, BTILES), FP32, kind="ExternalOutput").ap()
    tower(nc, t, out)
    r = run_bass_kernel_spmd(nc, [{f"in_{name}": a for name, a in arrays.items()}], core_ids=[0])
    return r.results[0]["out_y"].T.reshape(BATCH, 1)
```
